# Optimizing a Trainium2 kernel written in Bass

```python
import numpy as np
import jax
import jax.numpy as jnp

def _softmax(x, axis=-1):
    return jax.nn.softmax(x, axis=axis)

def _gelu(x):
    return jax.nn.gelu(x, approximate=True)

def _silu(x):
    return jax.nn.silu(x)

def _sigmoid(x):
    return jax.nn.sigmoid(x)

def _layernorm(x, axis=-1, eps=1e-05):
    m = jnp.mean(x, axis=axis, keepdims=True)
    v = jnp.var(x, axis=axis, keepdims=True)
    return (x - m) / jnp.sqrt(v + eps)

def _scatter_add(tgt, idx, src, axis=0):
    return tgt.at[idx].add(src)

def _segment_sum(src, seg, n):
    return jax.ops.segment_sum(src, seg, n)
kernel_name = 'mk_dlrm_tower_d1_rec_r8_250044'

def setup_inputs(seed: int=0):
    np.random.seed(seed)
    _w = jnp.asarray

    def _rec_inputs():
        import jax
        import jax.numpy as jnp
        _tk = jax.random.key(seed)
        dense_ctx = jax.random.normal(jax.random.fold_in(_tk, 190), (2048, 16), jnp.float32)
        ids = jnp.stack([jax.random.randint(jax.random.fold_in(_tk, 200 + f), (2048,), 0, v, jnp.int32) for f, v in enumerate([1250, 1250, 12500, 12500, 1000, 1250, 1000, 125000, 125000, 1250, 12500, 1000, 125000, 1250, 125000, 12500, 125000, 1000, 1250, 12500, 1000, 1250, 1250, 1000, 1250, 1250, 12500, 1000, 125000, 12500, 12500, 1000, 1250, 1000, 1250, 1000, 12500, 1000, 1250, 12500])], axis=1)
        tbl_0 = 0.05 * jax.random.normal(jax.random.fold_in(_tk, 500 + 0), (1250, 32), jnp.float32)
        tbl_1 = 0.05 * jax.random.normal(jax.random.fold_in(_tk, 500 + 1), (1250, 32), jnp.float32)
        tbl_2 = 0.05 * jax.random.normal(jax.random.fold_in(_tk, 500 + 2), (12500, 32), jnp.float32)
        tbl_3 = 0.05 * jax.random.normal(jax.random.fold_in(_tk, 500 + 3), (12500, 32), jnp.float32)
        tbl_4 = 0.05 * jax.random.normal(jax.random.fold_in(_tk, 500 + 4), (1000, 32), jnp.float32)
        tbl_5 = 0.05 * jax.random.normal(jax.random.fold_in(_tk, 500 + 5), (1250, 32), jnp.float32)
        tbl_6 = 0.05 * jax.random.normal(jax.random.fold_in(_tk, 500 + 6), (1000, 32), jnp.float32)
        tbl_7 = 0.05 * jax.random.normal(jax.random.fold_in(_tk, 500 + 7), (125000, 32), jnp.float32)
        tbl_8 = 0.05 * jax.random.normal(jax.random.fold_in(_tk, 500 + 8), (125000, 32), jnp.float32)
        tbl_9 = 0.05 * jax.random.normal(jax.random.fold_in(_tk, 500 + 9), (1250, 32), jnp.float32)
        tbl_10 = 0.05 * jax.random.normal(jax.random.fold_in(_tk, 500 + 10), (12500, 32), jnp.float32)
        tbl_11 = 0.05 * jax.random.normal(jax.random.fold_in(_tk, 500 + 11), (1000, 32), jnp.float32)
        tbl_12 = 0.05 * jax.random.normal(jax.random.fold_in(_tk, 500 + 12), (125000, 32), jnp.float32)
        tbl_13 = 0.05 * jax.random.normal(jax.random.fold_in(_tk, 500 + 13), (1250, 32), jnp.float32)
        tbl_14 = 0.05 * jax.random.normal(jax.random.fold_in(_tk, 500 + 14), (125000, 32), jnp.float32)
        tbl_15 = 0.05 * jax.random.normal(jax.random.fold_in(_tk, 500 + 15), (12500, 32), jnp.float32)
        tbl_16 = 0.05 * jax.random.normal(jax.random.fold_in(_tk, 500 + 16), (125000, 32), jnp.float32)
        tbl_17 = 0.05 * jax.random.normal(jax.random.fold_in(_tk, 500 + 17), (1000, 32), jnp.float32)
        tbl_18 = 0.05 * jax.random.normal(jax.random.fold_in(_tk, 500 + 18), (1250, 32), jnp.float32)
        tbl_19 = 0.05 * jax.random.normal(jax.random.fold_in(_tk, 500 + 19), (12500, 32), jnp.float32)
        tbl_20 = 0.05 * jax.random.normal(jax.random.fold_in(_tk, 500 + 20), (1000, 32), jnp.float32)
        tbl_21 = 0.05 * jax.random.normal(jax.random.fold_in(_tk, 500 + 21), (1250, 32), jnp.float32)
        tbl_22 = 0.05 * jax.random.normal(jax.random.fold_in(_tk, 500 + 22), (1250, 32), jnp.float32)
        tbl_23 = 0.05 * jax.random.normal(jax.random.fold_in(_tk, 500 + 23), (1000, 32), jnp.float32)
        tbl_24 = 0.05 * jax.random.normal(jax.random.fold_in(_tk, 500 + 24), (1250, 32), jnp.float32)
        tbl_25 = 0.05 * jax.random.normal(jax.random.fold_in(_tk, 500 + 25), (1250, 32), jnp.float32)
        tbl_26 = 0.05 * jax.random.normal(jax.random.fold_in(_tk, 500 + 26), (12500, 32), jnp.float32)
        tbl_27 = 0.05 * jax.random.normal(jax.random.fold_in(_tk, 500 + 27), (1000, 32), jnp.float32)
        tbl_28 = 0.05 * jax.random.normal(jax.random.fold_in(_tk, 500 + 28), (125000, 32), jnp.float32)
        tbl_29 = 0.05 * jax.random.normal(jax.random.fold_in(_tk, 500 + 29), (12500, 32), jnp.float32)
        tbl_30 = 0.05 * jax.random.normal(jax.random.fold_in(_tk, 500 + 30), (12500, 32), jnp.float32)
        tbl_31 = 0.05 * jax.random.normal(jax.random.fold_in(_tk, 500 + 31), (1000, 32), jnp.float32)
        tbl_32 = 0.05 * jax.random.normal(jax.random.fold_in(_tk, 500 + 32), (1250, 32), jnp.float32)
        tbl_33 = 0.05 * jax.random.normal(jax.random.fold_in(_tk, 500 + 33), (1000, 32), jnp.float32)
        tbl_34 = 0.05 * jax.random.normal(jax.random.fold_in(_tk, 500 + 34), (1250, 32), jnp.float32)
        tbl_35 = 0.05 * jax.random.normal(jax.random.fold_in(_tk, 500 + 35), (1000, 32), jnp.float32)
        tbl_36 = 0.05 * jax.random.normal(jax.random.fold_in(_tk, 500 + 36), (12500, 32), jnp.float32)
        tbl_37 = 0.05 * jax.random.normal(jax.random.fold_in(_tk, 500 + 37), (1000, 32), jnp.float32)
        tbl_38 = 0.05 * jax.random.normal(jax.random.fold_in(_tk, 500 + 38), (1250, 32), jnp.float32)
        tbl_39 = 0.05 * jax.random.normal(jax.random.fold_in(_tk, 500 + 39), (12500, 32), jnp.float32)
        _rk = jax.random.fold_in(_tk, 7)
        W_top1 = 0.0354441 * jax.random.normal(jax.random.fold_in(_tk, 801), (796, 512), jnp.float32)
        W_top2 = 0.0441942 * jax.random.normal(jax.random.fold_in(_tk, 802), (512, 256), jnp.float32)
        W_top3 = 0.0625 * jax.random.normal(jax.random.fold_in(_tk, 803), (256, 1), jnp.float32)
        b_top1 = jnp.zeros((512,), jnp.float32)
        b_top2 = jnp.zeros((256,), jnp.float32)
        return (dense_ctx, ids, tbl_0, tbl_1, tbl_2, tbl_3, tbl_4, tbl_5, tbl_6, tbl_7, tbl_8, tbl_9, tbl_10, tbl_11, tbl_12, tbl_13, tbl_14, tbl_15, tbl_16, tbl_17, tbl_18, tbl_19, tbl_20, tbl_21, tbl_22, tbl_23, tbl_24, tbl_25, tbl_26, tbl_27, tbl_28, tbl_29, tbl_30, tbl_31, tbl_32, tbl_33, tbl_34, tbl_35, tbl_36, tbl_37, tbl_38, tbl_39, W_top1, b_top1, W_top2, b_top2, W_top3)
    dense_ctx, ids, tbl_0, tbl_1, tbl_2, tbl_3, tbl_4, tbl_5, tbl_6, tbl_7, tbl_8, tbl_9, tbl_10, tbl_11, tbl_12, tbl_13, tbl_14, tbl_15, tbl_16, tbl_17, tbl_18, tbl_19, tbl_20, tbl_21, tbl_22, tbl_23, tbl_24, tbl_25, tbl_26, tbl_27, tbl_28, tbl_29, tbl_30, tbl_31, tbl_32, tbl_33, tbl_34, tbl_35, tbl_36, tbl_37, tbl_38, tbl_39, W_top1, b_top1, W_top2, b_top2, W_top3 = _rec_inputs()

    def _L0_rec_setup():
        import jax, jax.numpy as jnp
        import numpy as np
        NUM_FIELDS = 40
        _I_IDX, _J_IDX = np.triu_indices(NUM_FIELDS, k=1)
        key = jax.random.key(seed)
        k1, k2 = jax.random.split(key)
        batch, num_fields, embed_dim = (1024, NUM_FIELDS, 32)
        num_interactions = num_fields * (num_fields - 1) // 2
        embeddings = jax.random.normal(k1, (batch, num_fields, embed_dim), dtype=jnp.float32)
        W = jax.random.normal(k2, (num_interactions, embed_dim, embed_dim), dtype=jnp.float32)
        return {'embeddings': embeddings, 'W': W}
    _L0_rec_all = _L0_rec_setup()
    _L0_rec_in = {k: v for k, v in _L0_rec_all.items() if k in ('W',)}
    del _L0_rec_all
    return {'dense_ctx': dense_ctx, 'ids': ids, 'tbl_0': tbl_0, 'tbl_1': tbl_1, 'tbl_2': tbl_2, 'tbl_3': tbl_3, 'tbl_4': tbl_4, 'tbl_5': tbl_5, 'tbl_6': tbl_6, 'tbl_7': tbl_7, 'tbl_8': tbl_8, 'tbl_9': tbl_9, 'tbl_10': tbl_10, 'tbl_11': tbl_11, 'tbl_12': tbl_12, 'tbl_13': tbl_13, 'tbl_14': tbl_14, 'tbl_15': tbl_15, 'tbl_16': tbl_16, 'tbl_17': tbl_17, 'tbl_18': tbl_18, 'tbl_19': tbl_19, 'tbl_20': tbl_20, 'tbl_21': tbl_21, 'tbl_22': tbl_22, 'tbl_23': tbl_23, 'tbl_24': tbl_24, 'tbl_25': tbl_25, 'tbl_26': tbl_26, 'tbl_27': tbl_27, 'tbl_28': tbl_28, 'tbl_29': tbl_29, 'tbl_30': tbl_30, 'tbl_31': tbl_31, 'tbl_32': tbl_32, 'tbl_33': tbl_33, 'tbl_34': tbl_34, 'tbl_35': tbl_35, 'tbl_36': tbl_36, 'tbl_37': tbl_37, 'tbl_38': tbl_38, 'tbl_39': tbl_39, 'W_top1': W_top1, 'b_top1': b_top1, 'W_top2': W_top2, 'b_top2': b_top2, 'W_top3': W_top3, 'L0_rec_W': _L0_rec_in['W']}

def reference(dense_ctx, ids, tbl_0, tbl_1, tbl_2, tbl_3, tbl_4, tbl_5, tbl_6, tbl_7, tbl_8, tbl_9, tbl_10, tbl_11, tbl_12, tbl_13, tbl_14, tbl_15, tbl_16, tbl_17, tbl_18, tbl_19, tbl_20, tbl_21, tbl_22, tbl_23, tbl_24, tbl_25, tbl_26, tbl_27, tbl_28, tbl_29, tbl_30, tbl_31, tbl_32, tbl_33, tbl_34, tbl_35, tbl_36, tbl_37, tbl_38, tbl_39, W_top1, b_top1, W_top2, b_top2, W_top3, L0_rec_W):
    import jax
    import jax.numpy as jnp

    def _L0_rec_ref(embeddings, W):
        import jax, jax.numpy as jnp
        import numpy as np
        NUM_FIELDS = 40
        _I_IDX, _J_IDX = np.triu_indices(NUM_FIELDS, k=1)
        vi = embeddings[:, _I_IDX, :]
        vj = embeddings[:, _J_IDX, :]
        return jnp.einsum('bke,kef,bkf->bk', vi, W, vj)
    e = jnp.stack([tbl_0[ids[:, 0]], tbl_1[ids[:, 1]], tbl_2[ids[:, 2]], tbl_3[ids[:, 3]], tbl_4[ids[:, 4]], tbl_5[ids[:, 5]], tbl_6[ids[:, 6]], tbl_7[ids[:, 7]], tbl_8[ids[:, 8]], tbl_9[ids[:, 9]], tbl_10[ids[:, 10]], tbl_11[ids[:, 11]], tbl_12[ids[:, 12]], tbl_13[ids[:, 13]], tbl_14[ids[:, 14]], tbl_15[ids[:, 15]], tbl_16[ids[:, 16]], tbl_17[ids[:, 17]], tbl_18[ids[:, 18]], tbl_19[ids[:, 19]], tbl_20[ids[:, 20]], tbl_21[ids[:, 21]], tbl_22[ids[:, 22]], tbl_23[ids[:, 23]], tbl_24[ids[:, 24]], tbl_25[ids[:, 25]], tbl_26[ids[:, 26]], tbl_27[ids[:, 27]], tbl_28[ids[:, 28]], tbl_29[ids[:, 29]], tbl_30[ids[:, 30]], tbl_31[ids[:, 31]], tbl_32[ids[:, 32]], tbl_33[ids[:, 33]], tbl_34[ids[:, 34]], tbl_35[ids[:, 35]], tbl_36[ids[:, 36]], tbl_37[ids[:, 37]], tbl_38[ids[:, 38]], tbl_39[ids[:, 39]]], axis=1)
    z = _L0_rec_ref(e, L0_rec_W)
    z = z.reshape(z.shape[0], -1)
    h = jnp.concatenate([z, dense_ctx], axis=1)
    h = jnp.maximum(h @ W_top1 + b_top1, 0.0)
    h = jnp.maximum(h @ W_top2 + b_top2, 0.0)
    y = h @ W_top3
    return y

_drawn_inputs = setup_inputs


def setup_inputs(seed=0):
    import zlib

    import numpy as np

    out = dict(_drawn_inputs(seed))
    spreads = {'b_top1': (0.0, 0.1), 'b_top2': (0.0, 0.1)}
    factors = {}
    for name, (base, spread) in spreads.items():
        noise = np.random.default_rng([zlib.crc32(name.encode()), seed]).standard_normal(out[name].shape)
        drawn = base * np.exp(spread * noise) if base else spread * noise
        out[name] = jnp.asarray(drawn.astype(out[name].dtype))
    for name, factor in factors.items():
        out[name] = (out[name] * factor).astype(out[name].dtype)
    return out
```

```python
from contextlib import ExitStack

import concourse.bass as bass
from concourse import mybir

F32 = mybir.dt.float32
F32R = mybir.dt.float32r
I32 = mybir.dt.int32
U32 = mybir.dt.uint32
ALU = mybir.AluOpType
ACT = mybir.ActivationFunctionType

P = 128
BATCH, FIELDS, E, DENSE = 2048, 40, 32, 16
H1, H2 = 512, 256
B = 512
GROUPS = BATCH // B
ROW_TILES = B // P
FPC = P // E
CHUNKS = FIELDS // FPC


def first_field(c, c_i):
    return 1 if c_i == c else 0


UNITS = [(c, jj, c_i) for c in range(CHUNKS) for c_i in range(c + 1) for jj in range(first_field(c, c_i), FPC)]
N_UNITS = len(UNITS)
PAIRS = []
for _c in range(CHUNKS):
    for _ci in range(_c + 1):
        _n = UNITS.index((_c, first_field(_c, _ci), _ci))
        _left = FPC - first_field(_c, _ci)
        while _left:
            PAIRS.append((_n, min(2, _left)))
            _n, _left = _n + PAIRS[-1][1], _left - PAIRS[-1][1]
N_PAIRS = len(PAIRS)
SLOTS = 3
PAIRS_UP = -(-N_PAIRS // SLOTS) * SLOTS

Z_UNITS = P // FPC
TILE_PAIRS = [[]]
for _p, (_n, _count) in enumerate(PAIRS):
    if sum(PAIRS[q][1] for q in TILE_PAIRS[-1]) + _count > Z_UNITS:
        TILE_PAIRS.append([])
    TILE_PAIRS[-1].append(_p)
Z_TILES = len(TILE_PAIRS)
Z_LAST = Z_TILES - 1
TILE_STARTS = [tile[0] for tile in TILE_PAIRS]
TILE_ENDS = [tile[-1] for tile in TILE_PAIRS]


def z_place(n):
    t = sum(PAIRS[p][0] <= n for p in TILE_STARTS) - 1
    quads = 3 if t == Z_LAST else 4
    pos, quad = divmod(n - PAIRS[TILE_STARTS[t]][0], quads)
    assert pos < E // FPC
    return t, quad, pos


GATHER_SLOTS = 5
TURN_IDS = GATHER_SLOTS * FPC * ROW_TILES
FILLS = FPC + 1
GROUP_FILLS = CHUNKS * FILLS + 1

W_COLS = N_UNITS * P
W_PIECES = 10
PIECE = W_COLS // W_PIECES
STAGES = 3


def group_steps():
    steps = [("split", 0)] + [("fill", 0, f) for f in range(FILLS)]
    pair, waiting = 0, []
    for c in range(CHUNKS):
        for c_i in range(c + 1):
            if c + 1 < CHUNKS and c_i == max(0, c - FILLS):
                steps.append(("split", c + 1))
            mine = [pair, pair + 1]
            pair += 2
            steps += [("multiply", p) for p in mine]
            steps += [("add", p) for p in waiting]
            waiting = mine
            if c + 1 < CHUNKS:
                steps += [("fill", c + 1, f) for f in range(FILLS) if c_i == max(0, c - FILLS + 1 + f)]
    steps += [("add", p) for p in waiting]
    return steps


STEPS = group_steps()


def dlrm_kernel(nc, tables, ids, dense_t, w_int, w1, b1, w2, b2, w3, out):
    with ExitStack() as ctx:
        def sb(name, shape, dt=F32):
            return ctx.enter_context(nc.sbuf_tensor(name, shape, dt))

        def psum(name, shape):
            return ctx.enter_context(nc.psum_tensor(name, shape, F32))

        def sem(name):
            return ctx.enter_context(nc.semaphore(name))

        w_parts = sb("w_parts", [P, W_COLS], F32R)
        ej_parts = sb("ej_parts", [P, 2, FPC, B], F32R)
        e_t = sb("e_t", [P, CHUNKS, B])
        prod = sb("prod", [P, SLOTS, 2, B])
        z_t = sb("z_t", [P, Z_TILES, B])
        w1_sb = sb("w1_sb", [P, Z_TILES, H1])
        w2_sb = sb("w2_sb", [P, H1 // P, H2])
        w3_sb = sb("w3_sb", [P, H2 // P])
        b1_sb = sb("b1_sb", [P, H1 // P])
        b2_sb = sb("b2_sb", [P, H2 // P])
        rows = sb("rows", [P, GATHER_SLOTS, ROW_TILES * FPC, E])
        parts = sb("parts", [P, ROW_TILES * FPC, 2, 2, E], F32R)
        ids_all = sb("ids_all", [P, GROUPS * ROW_TILES * FIELDS], I32)
        ids_now = sb("ids_now", [P, ROW_TILES * FIELDS], I32)
        eye = sb("eye", [P, P])
        eye_r = sb("eye_r", [P, P], F32R)
        ones = sb("ones", [P, 2 * E - FPC])
        y_sb = sb("y_sb", [P, GROUPS * ROW_TILES])

        prod_flat = prod[:].rearrange("p s u b -> p (s u b)")
        h1_sb = prod_flat[:, 0:H1 // P * B].rearrange("p (m b) -> p m b", b=B)
        h2_sb = prod_flat[:, H1 // P * B:(H1 + H2) // P * B].rearrange("p (m b) -> p m b", b=B)
        y_rows = prod_flat[0:GROUPS * ROW_TILES, 0:P]
        stages = [prod_flat[:, 0:PIECE], z_t[:].rearrange("p t b -> p (t b)")[:, 0:PIECE],
                  e_t[:].rearrange("p c b -> p (c b)")[:, 0:PIECE]]

        u_ps = psum("u_ps", [P, 2 * SLOTS, B])
        z_ps = psum("z_ps", [P, B])
        turn_ps = psum("turn_ps", [P, B])

        s_ids = sem("s_ids")
        s_ids_now = sem("s_ids_now")
        s_blank = sem("s_blank")
        s_const = sem("s_const")
        s_ones_blank = sem("s_ones_blank")
        s_ones = sem("s_ones")
        s_eye_r = sem("s_eye_r")
        s_stage = [sem(f"s_stage{i}") for i in range(STAGES)]
        s_w_high = sem("s_w_high")
        s_w_split = sem("s_w_split")
        s_mlp_w = sem("s_mlp_w")
        s_z_blank = sem("s_z_blank")
        s_dense = sem("s_dense")
        s_rows = [sem(f"s_rows{i}") for i in range(GATHER_SLOTS)]
        s_slot_open = sem("s_slot_open")
        s_high = sem("s_high")
        s_low = sem("s_low")
        s_filled = sem("s_filled")
        s_drained = sem("s_drained")
        s_u = sem("s_u")
        s_prod = sem("s_prod")
        s_added = sem("s_added")
        s_z_out = sem("s_z_out")
        s_h1 = sem("s_h1")
        s_h1_relu = sem("s_h1_relu")
        s_h2 = sem("s_h2")
        s_h2_relu = sem("s_h2_relu")
        s_y_turned = sem("s_y_turned")
        s_y_rows = sem("s_y_rows")
        s_out = sem("s_out")

        N_M1, N_M2 = H1 // P, H2 // P
        block = ctx.enter_context(nc.Block())

        @block.sync
        def _(sp):
            sp.dma_start(ids_all[:], ids).then_inc(s_ids, 16)
            for q in range(W_PIECES):
                if q >= STAGES:
                    sp.wait_ge(s_w_split, q - STAGES + 1)
                for r in range(P // E):
                    sp.dma_start(stages[q % STAGES][E * r:E * r + E, :],
                                 w_int[:, PIECE * q:PIECE * (q + 1)]).then_inc(s_stage[q % STAGES], 16)
            sp.dma_start(w1_sb[:], w1).then_inc(s_mlp_w, 16)
            sp.dma_start(w2_sb[:], w2).then_inc(s_mlp_w, 16)
            sp.dma_start(w3_sb[:], w3).then_inc(s_mlp_w, 16)
            sp.dma_start(b1_sb[:], b1).then_inc(s_mlp_w, 16)
            sp.dma_start(b2_sb[:], b2).then_inc(s_mlp_w, 16)
            sp.wait_ge(s_z_blank, 1)
            dense_rows = z_t[3 * E:3 * E + DENSE, Z_LAST, :]
            sp.dma_start(dense_rows, dense_t[:, 0:B]).then_inc(s_dense, 16)
            with sp.Fori(1, GROUPS) as g:
                sp.wait_ge(s_h1, g * N_M1)
                sp.dma_start(dense_rows, dense_t[:, bass.ds(g * B, B)]).then_inc(s_dense, 16)
            sp.wait_ge(s_y_rows, 1)
            sp.dma_start(out, y_rows).then_inc(s_out, 16)
            sp.wait_ge(s_out, 16)

        @block.gpsimd
        def _(pool):
            pool.memset(eye[:], 0.0).then_inc(s_blank, 1)
            pool.wait_ge(s_blank, 1)
            pool.affine_select(out=eye[:], in_=eye[:], compare_op=ALU.not_equal, fill=1.0, base=0,
                               pattern=[[-1, P]], channel_multiplier=1).then_inc(s_const, 1)
            pool.wait_ge(s_ids, 16)
            with pool.Fori(0, GROUPS) as g:
                for c in range(CHUNKS):
                    turn, slot = divmod(c, GATHER_SLOTS)
                    if slot == 0:
                        pool.tensor_copy(ids_now[:, turn * TURN_IDS:(turn + 1) * TURN_IDS],
                                         ids_all[:, bass.ds(g * (ROW_TILES * FIELDS) + turn * TURN_IDS, TURN_IDS)]
                                         ).then_inc(s_ids_now, 1)
                        pool.wait_ge(s_ids_now, g * (CHUNKS // GATHER_SLOTS) + (turn + 1))
                    if c >= GATHER_SLOTS:
                        pool.wait_ge(s_filled, g * GROUP_FILLS + (GROUP_FILLS + (c - GATHER_SLOTS + 1) * FILLS))
                    else:
                        pool.wait_ge(s_filled, g * GROUP_FILLS + (c + CHUNKS - GATHER_SLOTS + 1) * FILLS)
                    pool.sem_inc(s_slot_open, 1)
                    for f in range(FPC):
                        for t in range(ROW_TILES):
                            at = (FPC * c + f) * ROW_TILES + t
                            pool.indirect_dma_start(
                                out=rows[:, slot, t * FPC + f, :], out_offset=None, in_=tables[FPC * c + f],
                                in_offset=bass.IndirectOffsetOnAxis(ap=ids_now[:, at:at + 1].bitcast(U32), axis=0),
                            ).then_inc(s_rows[slot], 16)

        @block.scalar
        def _(act):
            act.sem_inc(s_drained, 1)
            act.sem_inc(s_z_out, 1)
            act.wait_ge(s_const, 1)
            act.copy(eye_r[:], eye[:]).then_inc(s_eye_r, 1)
            for q in range(W_PIECES):
                act.wait_ge(s_stage[q % STAGES], 16 * (P // E) * (q // STAGES + 1))
                act.copy(w_parts[:, PIECE * q:PIECE * (q + 1)], stages[q % STAGES]).then_inc(s_w_high, 1)
            act.wait_ge(s_mlp_w, 5 * 16)
            with act.Fori(0, GROUPS) as g:
                for step in STEPS:
                    if step[0] == "split":
                        _, c = step
                        turn, slot = divmod(c, GATHER_SLOTS)
                        act.wait_ge(s_rows[slot], g * (16 * ROW_TILES * FPC * (CHUNKS // GATHER_SLOTS))
                                    + 16 * ROW_TILES * FPC * (turn + 1))
                        twice = rows[:, slot].unsqueeze(2).to_broadcast([P, ROW_TILES * FPC, 2, E])
                        act.copy(parts[:, :, :, 0, :], twice).then_inc(s_high, 1)
                    if step[0] == "fill":
                        _, c, f = step
                        act.wait_ge(s_filled, g * GROUP_FILLS + (GROUP_FILLS + c * FILLS + f + 1))
                        dst = ej_parts[:, c % 2, f, :] if f < FPC else e_t[:, c, :]
                        act.copy(dst, turn_ps[:]).then_inc(s_drained, 1)
                    if step[0] == "add":
                        p = step[1]
                        if p in TILE_ENDS:
                            t = TILE_ENDS.index(p)
                            top = 3 * E if t == Z_LAST else P
                            act.wait_ge(s_added, g * PAIRS_UP + (SLOTS + p + 1))
                            act.copy(z_t[0:top, t, :], z_ps[0:top, :]).then_inc(s_z_out, 1)
                for m in range(N_M1):
                    act.wait_ge(s_h1, g * N_M1 + (m + 1))
                    act.activation(h1_sb[:, m, :], u_ps[:, m, :], ACT.Relu, bias=b1_sb[:, m:m + 1]
                                   ).then_inc(s_h1_relu, 1)
                for m in range(N_M2):
                    act.wait_ge(s_h2, g * N_M2 + (m + 1))
                    act.activation(h2_sb[:, m, :], u_ps[:, N_M1 + m, :], ACT.Relu, bias=b2_sb[:, m:m + 1]
                                   ).then_inc(s_h2_relu, 1)
                act.wait_ge(s_filled, g * GROUP_FILLS + 2 * GROUP_FILLS)
                act.copy(y_sb[:, bass.ds(g * ROW_TILES, ROW_TILES)], turn_ps[:, 0:ROW_TILES]).then_inc(s_drained, 1)
            act.wait_ge(s_y_turned, 1)
            act.copy(y_rows, turn_ps[0:GROUPS * ROW_TILES, 0:P]).then_inc(s_y_rows, 1)

        @block.vector
        def _(dve):
            dve.sem_inc(s_prod, SLOTS)
            dve.memset(ones[:], 0.0).then_inc(s_ones_blank, 1)
            dve.wait_ge(s_ones_blank, 1)
            for m in range(FPC):
                dve.memset(ones[E * m:E * m + E, E - FPC + m:E - FPC + m + 1], 1.0).then_inc(s_ones, 1)
            dve.memset(z_t[3 * E:P, Z_LAST, :], 0.0).then_inc(s_z_blank, 1)
            half = slice(P // 2, P)
            for q in range(W_PIECES):
                dve.wait_ge(s_w_high, q + 1)
                w_q = w_parts[half, PIECE * q:PIECE * (q + 1)]
                dve.tensor_tensor(w_q, stages[q % STAGES][half, :], w_q.bitcast(F32), ALU.subtract
                                  ).then_inc(s_w_split, 1)
            with dve.Fori(0, GROUPS) as g:
                for step in STEPS:
                    if step[0] == "split":
                        _, c = step
                        slot = c % GATHER_SLOTS
                        dve.wait_ge(s_high, g * CHUNKS + (c + 1))
                        twice = rows[:, slot].unsqueeze(2).to_broadcast([P, ROW_TILES * FPC, 2, E])
                        dve.tensor_tensor(parts[:, :, :, 1, :], twice, parts[:, :, :, 0, :].bitcast(F32),
                                          ALU.subtract).then_inc(s_low, 1)
                    if step[0] == "multiply":
                        p = step[1]
                        first, count = PAIRS[p]
                        c, jj, c_i = UNITS[first]
                        slot = p % SLOTS
                        dve.wait_ge(s_u, g * N_PAIRS + (p + 1))
                        dve.wait_ge(s_added, g * PAIRS_UP + (p + 1))
                        if c_i == c:
                            dve.wait_ge(s_drained, g * GROUP_FILLS + (1 + (c + 1) * FILLS))
                        e_i = e_t[:, c_i:c_i + 1, :].to_broadcast([P, count, B])
                        dve.tensor_tensor(prod[:, slot, 0:count, :], u_ps[:, 2 * slot:2 * slot + count, :], e_i,
                                          ALU.mult).then_inc(s_prod, 1 if p < N_PAIRS - 1 else 1 + PAIRS_UP - N_PAIRS)

        @block.tensor
        def _(pe):
            pe.sem_inc(s_added, SLOTS)
            pe.sem_inc(s_filled, GROUP_FILLS)
            four_parts = parts[:].rearrange("p n a b e -> p n (a b e)")
            whole_rows = rows[:].rearrange("p s (t f) e -> p s t (f e)", f=FPC)
            pe.wait_ge(s_eye_r, 1)
            pe.wait_ge(s_ones, FPC)
            pe.wait_ge(s_w_split, W_PIECES)
            pe.wait_ge(s_mlp_w, 5 * 16)
            with pe.Fori(0, GROUPS) as g:
                for step in STEPS:
                    if step[0] == "fill":
                        _, c, f = step
                        if f == 0:
                            pe.wait_ge(s_low, g * CHUNKS + (c + 1))
                        pe.wait_ge(s_drained, g * GROUP_FILLS + (c * FILLS + f + 1))
                        for t in range(ROW_TILES):
                            cols = turn_ps[:, t * P:(t + 1) * P]
                            if f < FPC:
                                mm = pe.matmul(cols, four_parts[:, t * FPC + f, :], eye_r[:], start=True, stop=True)
                            else:
                                mm = pe.transpose(cols, whole_rows[:, c % GATHER_SLOTS, t, :], eye[:])
                        mm.then_inc(s_filled, 1)
                    if step[0] == "multiply":
                        p = step[1]
                        first, count = PAIRS[p]
                        slot = p % SLOTS
                        pe.wait_ge(s_prod, g * PAIRS_UP + (p + 1))
                        for u in range(count):
                            c, jj, c_i = UNITS[first + u]
                            if c_i == 0:
                                pe.wait_ge(s_drained, g * GROUP_FILLS + (1 + c * FILLS + jj + 1))
                            w = w_parts[:, P * (first + u):P * (first + u + 1)]
                            mm = pe.matmul(u_ps[:, 2 * slot + u, :], w, ej_parts[:, c % 2, jj, :],
                                           start=True, stop=True)
                        mm.then_inc(s_u, 1)
                    if step[0] == "add":
                        p = step[1]
                        first, count = PAIRS[p]
                        slot = p % SLOTS
                        pe.wait_ge(s_prod, g * PAIRS_UP + (SLOTS + p + 1))
                        for u in range(count):
                            n = first + u
                            t, quad, pos = z_place(n)
                            if u == 0 and p in TILE_STARTS:
                                pe.wait_ge(s_z_out, g * Z_TILES + (t + 1))
                            last_of_quad = not any(z_place(k)[:2] == (t, quad) for k in range(n + 1, N_UNITS))
                            mm = pe.matmul(z_ps[E * quad:E * quad + E, :],
                                           ones[:, E - FPC - FPC * pos:2 * E - FPC - FPC * pos],
                                           prod[:, slot, u, :], start=(pos == 0), stop=last_of_quad)
                        mm.then_inc(s_added, 1 if p < N_PAIRS - 1 else 1 + PAIRS_UP - N_PAIRS)
                pe.wait_ge(s_prod, g * PAIRS_UP + (SLOTS + PAIRS_UP))
                for m in range(N_M1):
                    for t in range(Z_LAST):
                        pe.matmul(u_ps[:, m, :], w1_sb[:, t, m * P:(m + 1) * P], z_t[:, t, :],
                                  start=(t == 0), stop=False)
                pe.wait_ge(s_z_out, g * Z_TILES + (Z_TILES + 1))
                pe.wait_ge(s_dense, g * 16 + 16)
                for m in range(N_M1):
                    pe.matmul(u_ps[:, m, :], w1_sb[:, Z_LAST, m * P:(m + 1) * P], z_t[:, Z_LAST, :],
                              start=False, stop=True).then_inc(s_h1, 1)
                for k in range(N_M1):
                    pe.wait_ge(s_h1_relu, g * N_M1 + (k + 1))
                    for m in range(N_M2):
                        mm = pe.matmul(u_ps[:, N_M1 + m, :], w2_sb[:, k, m * P:(m + 1) * P], h1_sb[:, k, :],
                                       start=(k == 0), stop=(k == N_M1 - 1))
                        if k == N_M1 - 1:
                            mm.then_inc(s_h2, 1)
                pe.wait_ge(s_h2_relu, g * N_M2 + N_M2)
                pe.wait_ge(s_drained, g * GROUP_FILLS + GROUP_FILLS)
                for t in range(ROW_TILES):
                    for k in range(N_M2):
                        mm = pe.matmul(turn_ps[:, t:t + 1], h2_sb[:, k, t * P:(t + 1) * P], w3_sb[:, k:k + 1],
                                       start=(k == 0), stop=(k == N_M2 - 1))
                mm.then_inc(s_filled, 1)
            pe.wait_ge(s_drained, GROUPS * GROUP_FILLS + 1)
            pe.matmul(turn_ps[0:GROUPS * ROW_TILES, 0:P], y_sb[:], eye[:], start=True, stop=True
                      ).then_inc(s_y_turned, 1)


def pair_index(i, j):
    return i * FIELDS - i * (i + 1) // 2 + j - i - 1


def unit_pairs():
    none = FIELDS * (FIELDS - 1) // 2
    return [[pair_index(FPC * c_i + s, FPC * c + jj) if FPC * c_i + s < FPC * c + jj else none
             for s in range(FPC)] for c, jj, c_i in UNITS]


def z_row_sources():
    pairs = FIELDS * (FIELDS - 1) // 2
    none = pairs + DENSE
    source = [[none] * Z_TILES for _ in range(P)]
    for n, four in enumerate(unit_pairs()):
        t, quad, pos = z_place(n)
        for s, k in enumerate(four):
            source[E * quad + FPC * pos + s][t] = k if k < pairs else none
    for d in range(DENSE):
        source[3 * E + d][Z_LAST] = pairs + d
    return source


def kernel(**inputs):
    import numpy as np
    import concourse.bacc as bacc
    from concourse.bass_utils import run_bass_kernel_spmd

    x = {k: np.asarray(v) for k, v in inputs.items()}
    w = np.concatenate([x["L0_rec_W"], np.zeros((1, E, E), np.float32)])
    w = w[np.array(unit_pairs()).reshape(-1)].transpose(2, 0, 1).reshape(E, W_COLS)
    w1 = np.concatenate([x["W_top1"], np.zeros((1, H1), np.float32)])[np.array(z_row_sources())]
    arrays = {
        "ids": x["ids"].reshape(GROUPS, ROW_TILES, P, FIELDS).transpose(2, 0, 3, 1).reshape(P, -1),
        "dense_t": x["dense_ctx"].T,
        "w_int": w,
        "w1": w1,
        "b1": x["b_top1"].reshape(H1 // P, P).T,
        "w2": x["W_top2"].reshape(H1 // P, P, H2).transpose(1, 0, 2),
        "b2": x["b_top2"].reshape(H2 // P, P).T,
        "w3": x["W_top3"].reshape(H2 // P, P).T,
    }
    for f in range(FIELDS):
        arrays[f"tbl_{f}"] = x[f"tbl_{f}"]
    arrays = {k: np.ascontiguousarray(v) for k, v in arrays.items()}

    nc = bacc.Bacc("TRN2", target_bir_lowering=False, num_devices=1)
    ap = {k: nc.dram_tensor(k, a.shape, mybir.dt.from_np(a.dtype), kind="ExternalInput").ap()
          for k, a in arrays.items()}
    y = nc.dram_tensor("y", (GROUPS * ROW_TILES, P), F32, kind="ExternalOutput").ap()
    dlrm_kernel(nc, [ap[f"tbl_{f}"] for f in range(FIELDS)], ap["ids"], ap["dense_t"], ap["w_int"],
                ap["w1"], ap["b1"], ap["w2"], ap["b2"], ap["w3"], y)
    r = run_bass_kernel_spmd(nc, [arrays], core_ids=[0])
    return r.results[0]["y"].reshape(BATCH, 1)
```

```python
from contextlib import ExitStack

import concourse.bass as bass
from concourse import mybir

F32 = mybir.dt.float32
F32R = mybir.dt.float32r
I32 = mybir.dt.int32
U32 = mybir.dt.uint32
ALU = mybir.AluOpType
ACT = mybir.ActivationFunctionType

P = 128
BATCH, FIELDS, E, DENSE = 2048, 40, 32, 16
H1, H2 = 512, 256
B = 512
GROUPS = BATCH // B
ROW_TILES = B // P
FPC = P // E
CHUNKS = FIELDS // FPC


def first_field(c, c_i):
    return 1 if c_i == c else 0


UNITS = [(c, jj, c_i) for c in range(CHUNKS) for c_i in range(c + 1) for jj in range(first_field(c, c_i), FPC)]
N_UNITS = len(UNITS)
PAIRS = []
for _c in range(CHUNKS):
    for _ci in range(_c + 1):
        _n = UNITS.index((_c, first_field(_c, _ci), _ci))
        _left = FPC - first_field(_c, _ci)
        while _left:
            PAIRS.append((_n, min(2, _left)))
            _n, _left = _n + PAIRS[-1][1], _left - PAIRS[-1][1]
N_PAIRS = len(PAIRS)
SLOTS = 3

Z_UNITS = P // FPC
TILE_PAIRS = [[]]
for _p, (_n, _count) in enumerate(PAIRS):
    if sum(PAIRS[q][1] for q in TILE_PAIRS[-1]) + _count > Z_UNITS:
        TILE_PAIRS.append([])
    TILE_PAIRS[-1].append(_p)
Z_TILES = len(TILE_PAIRS)
Z_LAST = Z_TILES - 1
TILE_STARTS = [tile[0] for tile in TILE_PAIRS]
TILE_ENDS = [tile[-1] for tile in TILE_PAIRS]


def z_place(n):
    t = sum(PAIRS[p][0] <= n for p in TILE_STARTS) - 1
    quads = 3 if t == Z_LAST else 4
    pos, quad = divmod(n - PAIRS[TILE_STARTS[t]][0], quads)
    assert pos < E // FPC
    return t, quad, pos


GATHER_SLOTS = 5
TURNS = CHUNKS // GATHER_SLOTS
SLOT_GATHERS = 16 * ROW_TILES * FPC
TURN_IDS = GATHER_SLOTS * FPC * ROW_TILES
EARLY = 3
EARLY_PAIRS = EARLY * (EARLY + 1)
FILLS = FPC + 1
MLP_SLOT = 2
TAIL_PAIR = 90


def psum_slot(p, last=False):
    p %= N_PAIRS
    return p % (2 if p < EARLY_PAIRS or last and p >= TAIL_PAIR else SLOTS)


def prod_slot(p):
    return p % N_PAIRS % SLOTS


def psum_before(p, last=False):
    return next(q for q in range(p - 1, p - N_PAIRS, -1) if psum_slot(q, last and q >= 0) == psum_slot(p, last))


def prod_before(p):
    return next(q for q in range(p - 1, p - N_PAIRS, -1) if prod_slot(q) == prod_slot(p))


W_COLS = N_UNITS * P
W_PIECES = 10
PIECE = W_COLS // W_PIECES
STAGES = 3
FIRST_PIECES = 4

TURN_SPREAD = 12
SPLIT_LEAD = 3
N_M1, N_M2 = H1 // P, H2 // P


def group_steps(last):
    end = N_PAIRS + (0 if last else EARLY_PAIRS)
    after = {p: [] for p in range(end)}

    def spread(steps, first, end):
        for k, step in enumerate(steps):
            after[first + k * (end - first) // len(steps)].append(step)

    def split_and_turn(c, split_at, first, end):
        after[split_at].append(("split", c))
        spread([("turn", c, f) for f in range(FILLS)], first, end)

    for c in range(EARLY + 1, CHUNKS):
        first, end_turn = c * (c - 1), c * (c + 1)
        begin = max(first + (1 if c == EARLY + 1 else SPLIT_LEAD), end_turn - TURN_SPREAD)
        if c > EARLY + 1:
            after[begin - SPLIT_LEAD].append(("split", c))
        spread([("turn", c, f) for f in range(FILLS)], begin, end_turn)
    steps = []
    if last:
        spread([("layer1", m, t) for t in range(Z_LAST - 1) for m in (1, 2)], TAIL_PAIR + 1, N_PAIRS - CHUNKS)
        spread([("layer1", 0, t) for t in range(Z_LAST)], N_PAIRS - 14, N_PAIRS)
        for p in range(EARLY_PAIRS, N_PAIRS):
            steps += [("multiply", p), ("add", p - SLOTS)] + after[p]
        return (steps + [("add", N_PAIRS - 3), ("layer1", 1, Z_LAST - 1), ("layer1", 2, Z_LAST - 1),
                         ("add", N_PAIRS - 2), ("layer1", 3, 0), ("add", N_PAIRS - 1)]
                + [("layer1", 3, t) for t in range(1, 3)] + [("layer1", m, Z_LAST) for m in range(3)]
                + [("layer1", 3, t) for t in range(3, Z_TILES)]
                + [("layer2", m, k) for k in range(N_M1) for m in range(N_M2)] + [("layer3",)])
    q = N_PAIRS
    split_and_turn(CHUNKS, q - 18, q - 16, q - 9)
    spread([("layer1", 0, t) for t in range(Z_LAST)], q - 7, q)
    after[q - 3].append(("split", CHUNKS + 1))
    for p in range(EARLY_PAIRS, q):
        steps += [("multiply", p), ("add", p - SLOTS)] + after[p]
    return steps + EARLY_STEPS


STEP_NAMES = {"S": "split", "T": "turn", "m": "multiply", "a": "add", "A": "layer1", "B": "layer2", "C": "layer3"}
NEXT = {"split": CHUNKS, "turn": CHUNKS, "multiply": N_PAIRS, "add": N_PAIRS}
EARLY_STEPS = [
    (STEP_NAMES[name[0]],) + tuple(int(x) + (NEXT.get(STEP_NAMES[name[0]], 0) if k == 0 else 0)
                                   for k, x in enumerate(name[1:].split(".")) if x)
    for name in """
    m0 a-3 A1.0 A1.1 m1 a-2 A1.2 a-1 A1.3 A1.4 A1.5 A0.6 A1.6
    A2.0 T1.0 A2.1 T1.1 A2.2 m2 T1.2 A2.3 a0 T1.3 A2.4 a1 m3 T1.4 A2.5 S2 m4 A2.6
    A3.0 a2 m5 T2.0 A3.1 a3 T2.1 A3.2 m6 T2.2 A3.3 a4 T2.3 A3.4 m7 a5 T2.4 A3.5 m8 S3 a6 A3.6
    m9 B0.0 a7 B0.1 T3.0 B0.2 m10 T3.1 B0.3 a8 B1.0 T3.2 B1.1 T3.3 B1.2 T3.4 B1.3 S4 m11 C""".split()]


def bank_uses(steps):
    return [s for s in steps if s[0] in ("turn", "layer3") or s == ("layer1", 0, Z_LAST)]


LOOP_STEPS = group_steps(False)
LAST_STEPS = group_steps(True)
LOOP_USES = bank_uses(LOOP_STEPS)
USES = len(LOOP_USES)
LAST_USES = bank_uses(LAST_STEPS)
FIRST_STEPS = [("w", q) for q in range(FIRST_PIECES)] + [("split", CHUNKS)] + [("turn", CHUNKS, f) for f in range(FILLS)]
for _step in LOOP_STEPS:
    if _step[0] == "split" and _step[1] > CHUNKS:
        _q = FIRST_PIECES * (_step[1] - CHUNKS)
        FIRST_STEPS += [("w", q) for q in range(_q, min(_q + FIRST_PIECES, W_PIECES))]
    if (_step[0] in ("split", "turn") and _step[1] > CHUNKS
            or _step[0] in ("multiply", "add") and _step[1] >= N_PAIRS):
        FIRST_STEPS.append(_step)
assert sum(count for _, count in PAIRS[:EARLY_PAIRS]) * P <= PIECE
FIRST_USES = [LOOP_USES.index(step) for step in bank_uses(FIRST_STEPS)]


def use_count(steps, step):
    if steps is not FIRST_STEPS:
        return 1
    use = LOOP_USES.index(step)
    return min([k for k in FIRST_USES if k > use] + [USES]) - use


assert all(LOOP_STEPS.index(("add", N_PAIRS + p)) > LOOP_STEPS.index(("layer1", N_M1 - 1, t))
           for t, p in enumerate(TILE_ENDS) if p < EARLY_PAIRS - SLOTS)
assert all(LOOP_STEPS.index(("layer1", 0, t)) > LOOP_STEPS.index(("add", p))
           for t, p in enumerate(TILE_ENDS) if p >= EARLY_PAIRS - SLOTS)
assert EARLY + 1 <= CHUNKS - N_M1
assert LAST_USES[:FILLS * (CHUNKS - EARLY - 1)] == LOOP_USES[:FILLS * (CHUNKS - EARLY - 1)]


def dlrm_kernel(nc, tables, ids, dense_t, w_int, w1, b1, w2, b2, w3, out):
    with ExitStack() as ctx:
        def sb(name, shape, dt=F32):
            return ctx.enter_context(nc.sbuf_tensor(name, shape, dt))

        def psum(name, shape):
            return ctx.enter_context(nc.psum_tensor(name, shape, F32))

        def sem(name):
            return ctx.enter_context(nc.semaphore(name))

        w_parts = sb("w_parts", [P, W_COLS], F32R)
        ej_parts = sb("ej_parts", [P, 2, FPC, B], F32R)
        e_t = sb("e_t", [P, CHUNKS, B])
        prod = sb("prod", [P, SLOTS, 2, B])
        z_t = sb("z_t", [P, Z_TILES, B])
        w1_sb = sb("w1_sb", [P, Z_TILES, H1])
        w2_sb = sb("w2_sb", [P, H1 // P, H2])
        w3_sb = sb("w3_sb", [P, H2 // P])
        b1_sb = sb("b1_sb", [P, H1 // P])
        b2_sb = sb("b2_sb", [P, H2 // P])
        rows = sb("rows", [P, GATHER_SLOTS, ROW_TILES * FPC, E])
        parts = sb("parts", [P, ROW_TILES * FPC, 2, 2, E], F32R)
        ids_all = sb("ids_all", [P, GROUPS * ROW_TILES * FIELDS], I32)
        ids_now = sb("ids_now", [P, ROW_TILES * FIELDS], I32)
        eye = sb("eye", [P, P])
        eye_r = sb("eye_r", [P, P], F32R)
        ones = sb("ones", [P, 2 * E - FPC])
        y_sb = sb("y_sb", [P, GROUPS * ROW_TILES])

        prod_flat = prod[:].rearrange("p s u b -> p (s u b)")
        h1_sb = e_t[:, CHUNKS - N_M1:CHUNKS, :]
        h2_sb = z_t[:, Z_LAST - N_M2:Z_LAST, :]
        y_rows = prod_flat[0:GROUPS * ROW_TILES, 0:P]
        stages = [z_t[:].rearrange("p t b -> p (t b)")[:, 0:PIECE],
                  e_t[:, EARLY + 1:].rearrange("p c b -> p (c b)")[:, 0:PIECE],
                  w1_sb[:].rearrange("p t h -> p (t h)")[:, 0:PIECE]]

        u_ps = psum("u_ps", [P, 2 * SLOTS, B])
        z_ps = psum("z_ps", [P, B])
        shared_ps = psum("shared_ps", [P, B])

        s_ids = sem("s_ids")
        s_ids_now = sem("s_ids_now")
        s_blank = sem("s_blank")
        s_const = sem("s_const")
        s_ones_blank = sem("s_ones_blank")
        s_ones = sem("s_ones")
        s_eye_r = sem("s_eye_r")
        s_stage = [sem(f"s_stage{i}") for i in range(STAGES)]
        s_w_high = sem("s_w_high")
        s_w_split = sem("s_w_split")
        s_mlp_w = sem("s_mlp_w")
        s_z_blank = sem("s_z_blank")
        s_dense = sem("s_dense")
        s_rows = [sem(f"s_rows{i}") for i in range(GATHER_SLOTS)]
        s_slot_open = sem("s_slot_open")
        s_high = sem("s_high")
        s_low = sem("s_low")
        s_parts = sem("s_parts")
        s_filled = sem("s_filled")
        s_drained = sem("s_drained")
        s_u = sem("s_u")
        s_prod = sem("s_prod")
        s_added = sem("s_added")
        s_z_out = sem("s_z_out")
        s_mlp = sem("s_mlp")
        s_mlp_relu = sem("s_mlp_relu")
        s_y_turned = sem("s_y_turned")
        s_y_rows = sem("s_y_rows")
        s_out = sem("s_out")

        def past(g, p):
            return g * N_PAIRS + (SLOTS + p + 1)

        def used(g, step, last=False):
            return g * USES + (2 * USES + (LAST_USES if last else LOOP_USES).index(step) + 1)

        def turned(g, c, f):
            if c <= EARLY:
                return g * USES + (USES + LOOP_USES.index(("turn", CHUNKS + c, f)) + 1)
            return used(g, ("turn", c, f))

        OWN = N_M1 - 1 + N_M2
        MLP_BANK = 2 * MLP_SLOT

        def own_tile(g, layer, m):
            return g * OWN + (m if layer == 1 else N_M1 + m)

        last_in_mlp_slot = max(p for p in range(N_PAIRS) if psum_slot(p, last=True) == MLP_SLOT)

        def layer1_ps(m, last):
            return shared_ps[:] if m == 0 else u_ps[:, [MLP_BANK, MLP_BANK + 1, 0 if last else MLP_BANK][m - 1], :]

        def layer2_ps(m, last):
            return u_ps[:, 2 + m if last else MLP_BANK + 1 - m, :]

        assert [psum_slot(N_PAIRS - k) for k in (3, 2, 1)] == [MLP_SLOT, 0, 1]

        block = ctx.enter_context(nc.Block())

        @block.sync
        def _(sp):
            sp.dma_start(ids_all[:], ids).then_inc(s_ids, 16)
            for q in range(W_PIECES):
                if q >= STAGES:
                    sp.wait_ge(s_w_split, q - STAGES + 1)
                for r in range(P // E):
                    sp.dma_start(stages[q % STAGES][E * r:E * r + E, :],
                                 w_int[:, PIECE * q:PIECE * (q + 1)]).then_inc(s_stage[q % STAGES], 16)
            sp.wait_ge(s_w_split, W_PIECES)
            sp.dma_start(w1_sb[:], w1).then_inc(s_mlp_w, 16)
            sp.dma_start(w2_sb[:], w2).then_inc(s_mlp_w, 16)
            sp.dma_start(w3_sb[:], w3).then_inc(s_mlp_w, 16)
            sp.dma_start(b1_sb[:], b1).then_inc(s_mlp_w, 16)
            sp.dma_start(b2_sb[:], b2).then_inc(s_mlp_w, 16)
            sp.wait_ge(s_z_blank, 1)
            dense_rows = z_t[3 * E:3 * E + DENSE, Z_LAST, :]
            sp.dma_start(dense_rows, dense_t[:, 0:B]).then_inc(s_dense, 16)
            with sp.Fori(1, GROUPS) as g:
                sp.wait_ge(s_mlp, g * OWN - N_M2)
                sp.dma_start(dense_rows, dense_t[:, bass.ds(g * B, B)]).then_inc(s_dense, 16)
            sp.wait_ge(s_y_rows, 1)
            sp.dma_start(out, y_rows).then_inc(s_out, 16)
            sp.wait_ge(s_out, 16)

        @block.gpsimd
        def _(pool):
            pool.memset(eye[:], 0.0).then_inc(s_blank, 1)
            pool.wait_ge(s_blank, 1)
            pool.affine_select(out=eye[:], in_=eye[:], compare_op=ALU.not_equal, fill=1.0, base=0,
                               pattern=[[-1, P]], channel_multiplier=1).then_inc(s_const, 1)
            pool.wait_ge(s_ids, 16)
            with pool.Fori(0, GROUPS) as g:
                for c in range(CHUNKS):
                    turn, slot = divmod(c, GATHER_SLOTS)
                    if slot == 0:
                        pool.tensor_copy(ids_now[:, turn * TURN_IDS:(turn + 1) * TURN_IDS],
                                         ids_all[:, bass.ds(g * (ROW_TILES * FIELDS) + turn * TURN_IDS, TURN_IDS)]
                                         ).then_inc(s_ids_now, 1)
                        pool.wait_ge(s_ids_now, g * TURNS + (turn + 1))
                    if c >= GATHER_SLOTS:
                        pool.wait_ge(s_filled, turned(g, c - GATHER_SLOTS, FILLS - 1))
                    else:
                        place = turned(-1, c + GATHER_SLOTS, FILLS - 1)
                        pool.wait_ge(s_filled, g * USES + place)
                    pool.sem_inc(s_slot_open, 1)
                    for f in range(FPC):
                        for t in range(ROW_TILES):
                            at = (FPC * c + f) * ROW_TILES + t
                            pool.indirect_dma_start(
                                out=rows[:, slot, t * FPC + f, :], out_offset=None, in_=tables[FPC * c + f],
                                in_offset=bass.IndirectOffsetOnAxis(ap=ids_now[:, at:at + 1].bitcast(U32), axis=0),
                            ).then_inc(s_rows[slot], 16)

        @block.scalar
        def _(act):
            act.sem_inc(s_drained, USES + FIRST_USES[0])
            act.sem_inc(s_z_out, 1)
            act.wait_ge(s_const, 1)
            act.copy(eye_r[:], eye[:]).then_inc(s_eye_r, 1)
            def split(g, c):
                turn, slot = divmod(c, GATHER_SLOTS)
                act.wait_ge(s_rows[slot], g * (SLOT_GATHERS * TURNS) + SLOT_GATHERS * (turn + 1))
                twice = rows[:, slot].unsqueeze(2).to_broadcast([P, ROW_TILES * FPC, 2, E])
                act.copy(parts[:, :, :, 0, :], twice).then_inc(s_high, 1)
                act.wait_ge(s_low, g * CHUNKS + (c + 1))
                act.copy(parts[:, :, 1, 1, :], parts[:, :, 0, 1, :]).then_inc(s_parts, 1)

            def run(g, steps, last=False):
                for step in steps:
                    if step[0] == "w":
                        q = step[1]
                        act.wait_ge(s_stage[q % STAGES], 16 * (P // E) * (q // STAGES + 1))
                        act.copy(w_parts[:, PIECE * q:PIECE * (q + 1)], stages[q % STAGES]).then_inc(s_w_high, 1)
                    if step[0] == "split":
                        split(g + step[1] // CHUNKS, step[1] % CHUNKS)
                    if step[0] == "turn":
                        _, c, f = step
                        act.wait_ge(s_filled, used(g, step, last))
                        dst = ej_parts[:, c % 2, f, :] if f < FPC else e_t[:, c % CHUNKS, :]
                        act.copy(dst, shared_ps[:]).then_inc(s_drained, use_count(steps, step))
                    if step[0] == "add" and step[1] % N_PAIRS in TILE_ENDS:
                        t = TILE_ENDS.index(step[1] % N_PAIRS)
                        top = 3 * E if t == Z_LAST else P
                        act.wait_ge(s_added, past(g, step[1]))
                        act.copy(z_t[0:top, t, :], z_ps[0:top, :]).then_inc(s_z_out, 1)
                    if step[0] == "layer1" and step[2] == Z_LAST:
                        m = step[1]
                        if m == 0:
                            act.wait_ge(s_filled, used(g, step, last))
                        else:
                            act.wait_ge(s_mlp, own_tile(g, 1, m))
                        act.activation(h1_sb[:, m, :], layer1_ps(m, last), ACT.Relu,
                                       bias=b1_sb[:, m:m + 1]).then_inc(s_mlp_relu if m > 0 else s_drained, 1)
                    if step[0] == "layer2" and step[2] == N_M1 - 1:
                        m = step[1]
                        act.wait_ge(s_mlp, own_tile(g, 2, m))
                        act.activation(h2_sb[:, m, :], layer2_ps(m, last), ACT.Relu,
                                       bias=b2_sb[:, m:m + 1]).then_inc(s_mlp_relu, 1)
                    if step[0] == "layer3":
                        act.wait_ge(s_filled, used(g, step, last))
                        act.copy(y_sb[:, bass.ds(g * ROW_TILES, ROW_TILES)], shared_ps[:, 0:ROW_TILES]
                                 ).then_inc(s_drained, 1)

            run(-1, FIRST_STEPS)
            act.wait_ge(s_mlp_w, 5 * 16)
            with act.Fori(0, GROUPS - 1) as g:
                run(g, LOOP_STEPS)
            run(GROUPS - 1, LAST_STEPS, last=True)
            act.wait_ge(s_y_turned, 1)
            act.copy(y_rows, shared_ps[0:GROUPS * ROW_TILES, 0:P]).then_inc(s_y_rows, 1)

        @block.vector
        def _(dve):
            dve.sem_inc(s_prod, SLOTS)
            dve.memset(ones[:], 0.0).then_inc(s_ones_blank, 1)
            dve.wait_ge(s_ones_blank, 1)
            for m in range(FPC):
                dve.memset(ones[E * m:E * m + E, E - FPC + m:E - FPC + m + 1], 1.0).then_inc(s_ones, 1)
            dve.memset(z_t[3 * E:P, Z_LAST, :], 0.0).then_inc(s_z_blank, 1)
            def split(g, c):
                dve.wait_ge(s_high, g * CHUNKS + (c + 1))
                dve.tensor_tensor(parts[:, :, 0, 1, :], rows[:, c % GATHER_SLOTS], parts[:, :, 0, 0, :].bitcast(F32),
                                  ALU.subtract).then_inc(s_low, 1)

            def run(g, steps, last=False):
                for step in steps:
                    if step[0] == "w":
                        q, half = step[1], slice(P // 2, P)
                        dve.wait_ge(s_w_high, q + 1)
                        w_q = w_parts[half, PIECE * q:PIECE * (q + 1)]
                        dve.tensor_tensor(w_q, stages[q % STAGES][half, :], w_q.bitcast(F32), ALU.subtract
                                          ).then_inc(s_w_split, 1)
                    if step[0] == "split":
                        split(g + step[1] // CHUNKS, step[1] % CHUNKS)
                    if step[0] == "multiply":
                        p = step[1]
                        first, count = PAIRS[p % N_PAIRS]
                        c, jj, c_i = UNITS[first]
                        in_psum = 2 * psum_slot(p, last)
                        dve.wait_ge(s_u, g * N_PAIRS + (p + 1))
                        dve.wait_ge(s_added, past(g, prod_before(p)))
                        if c_i == c:
                            dve.wait_ge(s_drained, turned(g + p // N_PAIRS, c, FPC))
                        e_i = e_t[:, c_i:c_i + 1, :].to_broadcast([P, count, B])
                        dve.tensor_tensor(prod[:, prod_slot(p), 0:count, :], u_ps[:, in_psum:in_psum + count, :], e_i,
                                          ALU.mult).then_inc(s_prod, 1)

            run(-1, FIRST_STEPS)
            with dve.Fori(0, GROUPS - 1) as g:
                run(g, LOOP_STEPS)
            run(GROUPS - 1, LAST_STEPS, last=True)

        @block.tensor
        def _(pe):
            pe.sem_inc(s_added, SLOTS)
            pe.sem_inc(s_filled, USES + FIRST_USES[0])
            four_parts = parts[:].rearrange("p n a b e -> p n (a b e)")
            whole_rows = rows[:].rearrange("p s (t f) e -> p s t (f e)", f=FPC)
            pe.wait_ge(s_eye_r, 1)
            pe.wait_ge(s_ones, FPC)
            pe.wait_ge(s_w_split, 1)

            def run(g, steps, last=False):
                def shared_free(step):
                    pe.wait_ge(s_drained, g * USES + (2 * USES + (LAST_USES if last else LOOP_USES).index(step)))

                for step in steps:
                    if step[0] == "turn":
                        _, c, f = step
                        if f == 0:
                            pe.wait_ge(s_parts, (g + c // CHUNKS) * CHUNKS + (c % CHUNKS + 1))
                        shared_free(step)
                        for t in range(ROW_TILES):
                            cols = shared_ps[:, t * P:(t + 1) * P]
                            if f < FPC:
                                mm = pe.matmul(cols, four_parts[:, t * FPC + f, :], eye_r[:], start=True, stop=True)
                            else:
                                mm = pe.transpose(cols, whole_rows[:, c % CHUNKS % GATHER_SLOTS, t, :], eye[:])
                        mm.then_inc(s_filled, use_count(steps, step))
                    if step[0] == "multiply":
                        p = step[1]
                        first, count = PAIRS[p % N_PAIRS]
                        in_psum = 2 * psum_slot(p, last)
                        pe.wait_ge(s_prod, past(g, psum_before(p, last)))
                        for u in range(count):
                            c, jj, c_i = UNITS[first + u]
                            if c_i == 0:
                                pe.wait_ge(s_drained, turned(g + p // N_PAIRS, c, jj))
                            w = w_parts[:, P * (first + u):P * (first + u + 1)]
                            mm = pe.matmul(u_ps[:, in_psum + u, :], w, ej_parts[:, c % 2, jj, :],
                                           start=True, stop=True)
                        mm.then_inc(s_u, 1)
                    if step[0] == "add":
                        p = step[1]
                        first, count = PAIRS[p % N_PAIRS]
                        pe.wait_ge(s_prod, past(g, p))
                        for u in range(count):
                            n = first + u
                            t, quad, pos = z_place(n)
                            if u == 0 and p % N_PAIRS in TILE_STARTS:
                                pe.wait_ge(s_z_out, (g + p // N_PAIRS) * Z_TILES + (t + 1))
                            last_of_quad = not any(z_place(k)[:2] == (t, quad) for k in range(n + 1, N_UNITS))
                            mm = pe.matmul(z_ps[E * quad:E * quad + E, :],
                                           ones[:, E - FPC - FPC * pos:2 * E - FPC - FPC * pos],
                                           prod[:, prod_slot(p), u, :], start=(pos == 0), stop=last_of_quad)
                        mm.then_inc(s_added, 1)
                    if step[0] == "layer1":
                        _, m, t = step
                        if t == 0 and m == 0:
                            shared_free((step[0], m, Z_LAST))
                        elif t == 0 and m == 3 and last:
                            pe.wait_ge(s_prod, past(g, N_PAIRS - 2))
                        elif t == 0 and m == 3:
                            pe.wait_ge(s_mlp_relu, own_tile(g, 1, 1))
                        elif t == 0:
                            pe.wait_ge(s_prod, past(g, last_in_mlp_slot if last else N_PAIRS - 3))
                        pe.wait_ge(s_z_out, g * Z_TILES + (t + 2))
                        if t == Z_LAST:
                            pe.wait_ge(s_dense, g * 16 + 16)
                        mm = pe.matmul(layer1_ps(m, last), w1_sb[:, t, m * P:(m + 1) * P],
                                       z_t[:, t, :], start=(t == 0), stop=(t == Z_LAST))
                        if t == Z_LAST:
                            mm.then_inc(s_filled if m == 0 else s_mlp, 1)
                    if step[0] == "layer2":
                        _, m, k = step
                        if m == 0 and k == 0:
                            pe.wait_ge(s_drained, used(g, ("layer1", 0, Z_LAST), last))
                        elif m == 0:
                            pe.wait_ge(s_mlp_relu, own_tile(g, 1, k))
                        if k == 0 and last:
                            pe.wait_ge(s_prod, past(g, N_PAIRS - 1))
                        elif k == 0:
                            pe.wait_ge(s_mlp_relu, own_tile(g, 1, 2 + m))
                        mm = pe.matmul(layer2_ps(m, last), w2_sb[:, k, m * P:(m + 1) * P],
                                       h1_sb[:, k, :], start=(k == 0), stop=(k == N_M1 - 1))
                        if k == N_M1 - 1:
                            mm.then_inc(s_mlp, 1)
                    if step[0] == "layer3":
                        pe.wait_ge(s_mlp_relu, own_tile(g, 2, N_M2 - 1))
                        shared_free(step)
                        for t in range(ROW_TILES):
                            for k in range(N_M2):
                                mm = pe.matmul(shared_ps[:, t:t + 1], h2_sb[:, k, t * P:(t + 1) * P],
                                               w3_sb[:, k:k + 1], start=(k == 0), stop=(k == N_M2 - 1))
                        mm.then_inc(s_filled, 1)

            run(-1, FIRST_STEPS)
            pe.wait_ge(s_w_split, W_PIECES)
            pe.wait_ge(s_mlp_w, 5 * 16)
            with pe.Fori(0, GROUPS - 1) as g:
                run(g, LOOP_STEPS)
            run(GROUPS - 1, LAST_STEPS, last=True)
            pe.wait_ge(s_drained, used(GROUPS - 1, ("layer3",), last=True))
            pe.matmul(shared_ps[0:GROUPS * ROW_TILES, 0:P], y_sb[:], eye[:], start=True, stop=True
                      ).then_inc(s_y_turned, 1)


def pair_index(i, j):
    return i * FIELDS - i * (i + 1) // 2 + j - i - 1


def unit_pairs():
    none = FIELDS * (FIELDS - 1) // 2
    return [[pair_index(FPC * c_i + s, FPC * c + jj) if FPC * c_i + s < FPC * c + jj else none
             for s in range(FPC)] for c, jj, c_i in UNITS]


def z_row_sources():
    pairs = FIELDS * (FIELDS - 1) // 2
    none = pairs + DENSE
    source = [[none] * Z_TILES for _ in range(P)]
    for n, four in enumerate(unit_pairs()):
        t, quad, pos = z_place(n)
        for s, k in enumerate(four):
            source[E * quad + FPC * pos + s][t] = k if k < pairs else none
    for d in range(DENSE):
        source[3 * E + d][Z_LAST] = pairs + d
    return source


def kernel(**inputs):
    import numpy as np
    import concourse.bacc as bacc
    from concourse.bass_utils import run_bass_kernel_spmd

    x = {k: np.asarray(v) for k, v in inputs.items()}
    w = np.concatenate([x["L0_rec_W"], np.zeros((1, E, E), np.float32)])
    w = w[np.array(unit_pairs()).reshape(-1)].transpose(2, 0, 1).reshape(E, W_COLS)
    w1 = np.concatenate([x["W_top1"], np.zeros((1, H1), np.float32)])[np.array(z_row_sources())]
    arrays = {
        "ids": x["ids"].reshape(GROUPS, ROW_TILES, P, FIELDS).transpose(2, 0, 3, 1).reshape(P, -1),
        "dense_t": x["dense_ctx"].T,
        "w_int": w,
        "w1": w1,
        "b1": x["b_top1"].reshape(H1 // P, P).T,
        "w2": x["W_top2"].reshape(H1 // P, P, H2).transpose(1, 0, 2),
        "b2": x["b_top2"].reshape(H2 // P, P).T,
        "w3": x["W_top3"].reshape(H2 // P, P).T,
    }
    for f in range(FIELDS):
        arrays[f"tbl_{f}"] = x[f"tbl_{f}"]
    arrays = {k: np.ascontiguousarray(v) for k, v in arrays.items()}

    nc = bacc.Bacc("TRN2", target_bir_lowering=False, num_devices=1)
    ap = {k: nc.dram_tensor(k, a.shape, mybir.dt.from_np(a.dtype), kind="ExternalInput").ap()
          for k, a in arrays.items()}
    y = nc.dram_tensor("y", (GROUPS * ROW_TILES, P), F32, kind="ExternalOutput").ap()
    dlrm_kernel(nc, [ap[f"tbl_{f}"] for f in range(FIELDS)], ap["ids"], ap["dense_t"], ap["w_int"],
                ap["w1"], ap["b1"], ap["w2"], ap["b2"], ap["w3"], y)
    r = run_bass_kernel_spmd(nc, [arrays], core_ids=[0])
    return r.results[0]["y"].reshape(BATCH, 1)
```
